# Optimizing a Trainium2 kernel written in Bass

```python
import numpy as np
import jax
import jax.numpy as jnp

def _softmax(x, axis=-1):
    return jax.nn.softmax(x, axis=axis)

def _gelu(x):
    return jax.nn.gelu(x, approximate=True)

def _silu(x):
    return jax.nn.silu(x)

def _sigmoid(x):
    return jax.nn.sigmoid(x)

def _layernorm(x, axis=-1, eps=1e-05):
    m = jnp.mean(x, axis=axis, keepdims=True)
    v = jnp.var(x, axis=axis, keepdims=True)
    return (x - m) / jnp.sqrt(v + eps)

def _scatter_add(tgt, idx, src, axis=0):
    return tgt.at[idx].add(src)

def _segment_sum(src, seg, n):
    return jax.ops.segment_sum(src, seg, n)
kernel_name = 'mk_rec_standalone_d1_rec_r8_6679c5'

def setup_inputs(seed: int=0):
    np.random.seed(seed)
    _w = jnp.asarray

    def _rec_inputs():
        import jax
        import jax.numpy as jnp
        _rk = jax.random.key(seed)
        r_x = 0.00021031 + 1.00007 * jax.random.normal(jax.random.fold_in(_rk, 1), (2048, 64, 128), jnp.float32)
        return r_x
    r_x = _rec_inputs()

    def _L0_rec_setup():
        import jax, jax.numpy as jnp
        import numpy as np
        NUM_FEATURES = 64
        _IU, _JU = np.triu_indices(NUM_FEATURES, k=1)
        key = jax.random.key(seed)
        x = jax.random.normal(key, (512, NUM_FEATURES, 128), dtype=jnp.float32)
        return {'x': x}
    _L0_rec_all = _L0_rec_setup()
    _L0_rec_in = {k: v for k, v in _L0_rec_all.items() if k in ()}
    del _L0_rec_all
    return {'r_x': r_x}

def reference(r_x):
    import jax
    import jax.numpy as jnp

    def _L0_rec_ref(x):
        import jax, jax.numpy as jnp
        import numpy as np
        NUM_FEATURES = 64
        _IU, _JU = np.triu_indices(NUM_FEATURES, k=1)
        gram = jnp.einsum('bfd,bgd->bfg', x, x)
        return gram[:, _IU, _JU]
    y = _L0_rec_ref(r_x)
    return y

_drawn_inputs = setup_inputs


def setup_inputs(seed=0):
    import zlib

    import numpy as np

    out = dict(_drawn_inputs(seed))
    spreads = {}
    factors = {}
    for name, (base, spread) in spreads.items():
        noise = np.random.default_rng([zlib.crc32(name.encode()), seed]).standard_normal(out[name].shape)
        drawn = base * np.exp(spread * noise) if base else spread * noise
        out[name] = jnp.asarray(drawn.astype(out[name].dtype))
    for name, factor in factors.items():
        out[name] = (out[name] * factor).astype(out[name].dtype)
    return out
```

```python
def build(nc, x, out):
    import concourse.mybir as mybir
    from contextlib import ExitStack

    fp32 = mybir.dt.float32
    ALU = mybir.AluOpType
    P = 128
    BLK = 32
    B, F, D = x.shape
    NOUT = out.shape[1]
    FPP = 8
    UB = P * FPP // F
    PAIRS = UB // 2
    UNITS = B // UB
    GU = BLK // PAIRS
    GROUPS = UNITS // GU
    SG = 2
    STORES = GROUPS // SG
    SU = SG * GU
    HF = F // 2

    XS, TS, XTS, QS = 8, 2, 4, 2
    BODY = 2 * SU
    TURNS = UNITS // BODY
    GB = BODY // GU
    SB = BODY // SU

    N0 = sum(F - 1 - i for i in range(HF))
    N1 = NOUT - N0

    PIECES = [(half, i, 2) for i in range(0, HF - 2, 2) for half in (0, 1)]
    PIECES += [(0, HF - 2, 1), (1, HF - 2, 1), (0, HF - 1, 1)]

    x_units = x.rearrange("(u b) (g t) d -> u (b g) (t d)", b=UB, t=FPP)
    out_turns = out.rearrange("(a g b h) n -> a h b g n", g=GB, b=BLK, h=2)

    with ExitStack() as ctx:
        def sb(name, shape):
            return ctx.enter_context(nc.sbuf_tensor(name, shape, fp32))

        def sem(name):
            return ctx.enter_context(nc.semaphore(name))

        x_sb = sb("x_sb", [P, XS, FPP * D])
        xt_sb = sb("xt_sb", [P, XTS, UB * F])
        square = sb("square", [P, QS, SG, HF * F])
        upper = sb("upper", [P, QS, SG, N0])
        lower = sb("lower", [P, QS, SG, N1])
        ident = sb("ident", [P, P])
        xt_ps = ctx.enter_context(nc.psum_tensor("xt_ps", [P, TS, FPP, P], fp32))
        gram_ps = ctx.enter_context(nc.psum_tensor("gram_ps", [P, BLK, F], fp32))

        ident_zeroed = sem("ident_zeroed")
        ident_ready = sem("ident_ready")
        loaded = [sem(f"loaded{s}") for s in range(XS)]
        transposed = sem("transposed")
        moved = sem("moved")
        grams = sem("grams")
        swapped = sem("swapped")
        packed = sem("packed")
        stored = [sem(f"stored{s}") for s in range(QS)]

        block = ctx.enter_context(nc.Block())

        def first(turn):
            return isinstance(turn, int) and turn == 0

        def turns(eng, body):
            body(0)
            with eng.Fori(1, TURNS) as turn:
                body(turn)

        @block.gpsimd
        def _(pool):
            nc.gpsimd.memset(ident[:, :], 0.0).then_inc(ident_zeroed, 1)
            pool.wait_ge(ident_zeroed, 1)
            nc.gpsimd.affine_select(out=ident[:, :], in_=ident[:, :], compare_op=ALU.not_equal, fill=1.0,
                                    base=0, pattern=[[-1, P]], channel_multiplier=1).then_inc(ident_ready, 1)

        @block.sync
        def _(sp):
            def body(turn):
                for k in range(BODY):
                    if not (first(turn) and k < XS):
                        sp.wait_ge(transposed, turn * BODY + k - XS + 1)
                    sp.dma_start(x_sb[:, k % XS, :], x_units[turn * BODY + k]).then_inc(loaded[k % XS], 16)

            turns(sp, body)

        @block.tensor
        def _(pe):
            def transpose_unit(turn, k):
                pe.wait_ge(loaded[k % XS], 16 * (turn * (BODY // XS) + k // XS + 1))
                if not (first(turn) and k < TS):
                    pe.wait_ge(moved, turn * BODY + k - TS + 1)
                for t in range(FPP):
                    last = nc.tensor.transpose(xt_ps[:, k % TS, t, :], x_sb[:, k % XS, t * D:(t + 1) * D],
                                               ident[:, :])
                last.then_inc(transposed, 1)

            def gram_unit(turn, k):
                pe.wait_ge(moved, turn * BODY + k + 1)
                if k % GU == 0 and not (first(turn) and turn * BODY + k < GU):
                    pe.wait_ge(swapped, turn * GB + k // GU)
                for m in range(PAIRS):
                    pair = k % GU * PAIRS + m
                    for h in range(2):
                        xb = xt_sb[:, k % XTS, (2 * m + h) * F:(2 * m + h + 1) * F]
                        last = nc.tensor.matmul(gram_ps[h * F:(h + 1) * F, pair, :], xb, xb, start=True, stop=True)
                last.then_inc(grams, 1)

            def body(turn):
                for k in range(BODY):
                    transpose_unit(turn, k)
                    if k > 0:
                        gram_unit(turn, k - 1)
                    elif not first(turn):
                        gram_unit(turn - 1, BODY - 1)

            pe.wait_ge(ident_ready, 1)
            turns(pe, body)
            gram_unit(TURNS - 1, BODY - 1)

        @block.scalar
        def _(act):
            def move_unit(turn, k):
                act.wait_ge(transposed, turn * BODY + k + 1)
                if not (first(turn) and turn * BODY + k < XTS):
                    act.wait_ge(grams, turn * BODY + k - XTS + 1)
                nc.scalar.copy(xt_sb[:, k % XTS, :].rearrange("d (c t) -> d t c", t=FPP),
                               xt_ps[:, k % TS, :, :]).then_inc(moved, 1)

            def store(turn, s):
                act.wait_ge(packed, (turn * SB + s + 1) * len(PIECES))
                for h in range(2):
                    for half, rows, cols in ((0, upper, slice(0, N0)), (1, lower, slice(N0, NOUT))):
                        p0 = h * F + half * HF
                        n = cols.stop - cols.start
                        dst = out_turns[turn, h, :, s * SG:(s + 1) * SG, cols]
                        act.dma_start(dst, rows[p0:p0 + BLK, s, :, 0:n]).then_inc(stored[s], 16)

            def body(turn):
                for k in range(BODY):
                    move_unit(turn, k)
                    if k % SU == SU // 2 and not first(turn):
                        store(turn - 1, k // SU)

            turns(act, body)
            for s in range(SB):
                store(TURNS - 1, s)
            for s in range(QS):
                act.wait_ge(stored[s], TURNS * 64)

        @block.vector
        def _(dve):
            def swap_group(turn, g):
                dve.wait_ge(grams, (turn * GB + g + 1) * GU)
                s, a = g // SG % QS, g % SG
                if a == 0 and not first(turn):
                    dve.wait_ge(packed, (turn * SB + s - 1) * len(PIECES))
                nc.vector.transpose(square[:, s, a, :].rearrange("p (i j) -> p j i", j=F),
                                    gram_ps[:, :, :].rearrange("p b j -> p j b")).then_inc(swapped, 1)

            def pack(turn, s, part, parts):
                if part == 0:
                    dve.wait_ge(swapped, (turn * SB + s + 1) * SG)
                    if not first(turn):
                        dve.wait_ge(stored[s], turn * 64)
                for n_piece in range(part * len(PIECES) // parts, (part + 1) * len(PIECES) // parts):
                    half, i, count = PIECES[n_piece]
                    rows, j0 = ((upper, 0), (lower, HF))[half]
                    done = (turn * SB + s) * len(PIECES) + n_piece - 1
                    if not (first(turn) and done <= 0):
                        dve.wait_ge(packed, done)
                    n = F - 1 - j0 - i
                    at = sum(F - 1 - j0 - r for r in range(i))
                    start = i * F + j0 + i + 1
                    if count == 1:
                        src = square[:, s, :, start:start + n]
                        dst = rows[:, s, :, at:at + n]
                    else:
                        src = square[:, s, :, start:start + 2 * (F + 1)].rearrange("p a (r j) -> p a r j", r=2)[:, :, :, 0:n]
                        dst = rows[:, s, :, at:at + 2 * n].rearrange("p a (r j) -> p a r j", r=2)
                    nc.vector.tensor_copy(dst, src).then_inc(packed, 1)

            def body(turn):
                for s in range(SB):
                    for a in range(SG):
                        swap_group(turn, s * SG + a)
                        if s > 0:
                            pack(turn, s - 1, a, SG)
                        elif not first(turn):
                            pack(turn - 1, SB - 1, a, SG)

            turns(dve, body)
            pack(TURNS - 1, SB - 1, 0, 1)


_IN = "r_x"


def kernel(**inputs):
    import numpy as np
    import concourse.bacc as bacc
    from concourse import mybir
    from concourse.bass_utils import run_bass_kernel_spmd

    a = np.ascontiguousarray(inputs[_IN])
    batches, features, _ = a.shape
    nc = bacc.Bacc("TRN2", target_bir_lowering=False, num_devices=1)
    x = nc.dram_tensor("x", a.shape, mybir.dt.float32, kind="ExternalInput").ap()
    out = nc.dram_tensor("out", (batches, features * (features - 1) // 2), mybir.dt.float32,
                         kind="ExternalOutput").ap()
    build(nc, x, out)
    r = run_bass_kernel_spmd(nc, [{"x": a}], core_ids=[0])
    return r.results[0]["out"]
```

```python
def build(nc, x, out):
    import concourse.mybir as mybir
    from contextlib import ExitStack

    fp32 = mybir.dt.float32
    ALU = mybir.AluOpType
    P = 128
    BLK = 32
    B, F, D = x.shape
    NOUT = out.shape[1]
    FPP = 8
    UB = P * FPP // F
    PAIRS = UB // 2
    UNITS = B // UB
    GU = BLK // PAIRS
    SG = 2
    SU = SG * GU
    STORES = UNITS // SU
    HF = F // 2
    TH = FPP // 2

    XS, TS, XTS, QS = 8, 4, 8, 2
    BODY = QS * SU
    TURNS = UNITS // BODY
    assert BODY % XS == BODY % XTS == 0 and UNITS == TURNS * BODY
    BG = BODY // GU
    BS = BODY // SU

    AHEAD = (2, 9, 10, 10, 10)
    assert AHEAD[-1] - AHEAD[0] == 2 * GU

    N0 = sum(F - 1 - i for i in range(HF))
    N1 = NOUT - N0
    PIECES = [(half, i, 2) for i in range(0, HF - 2, 2) for half in (0, 1)]
    PIECES += [(0, HF - 2, 1), (1, HF - 2, 1), (0, HF - 1, 1)]
    NP = len(PIECES)

    x_units = x.rearrange("(u b) (g t) d -> u (b g) (t d)", b=UB, t=FPP)
    out_stores = out.rearrange("(s g b h) n -> s h b g n", g=SG, b=BLK, h=2)

    with ExitStack() as ctx:
        def sb(name, shape):
            return ctx.enter_context(nc.sbuf_tensor(name, shape, fp32))

        def sem(name):
            return ctx.enter_context(nc.semaphore(name))

        x_sb = sb("x_sb", [P, XS, FPP * D])
        xt_sb = sb("xt_sb", [P, XTS, UB * F])
        square = sb("square", [P, QS, SG, HF * F])
        upper = sb("upper", [P, QS, SG, N0])
        lower = sb("lower", [P, QS, SG, N1])
        ident = sb("ident", [P, P])
        xt_ps = ctx.enter_context(nc.psum_tensor("xt_ps", [P, TS, TH, P], fp32))
        gram_ps = ctx.enter_context(nc.psum_tensor("gram_ps", [P, BLK, F], fp32))

        ident_zeroed = sem("ident_zeroed")
        ident_ready = sem("ident_ready")
        loaded = [sem(f"loaded{s}") for s in range(XS)]
        transposed = sem("transposed")
        moved = sem("moved")
        grams = sem("grams")
        swapped = sem("swapped")
        packed = sem("packed")
        stored = [sem(f"stored{s}") for s in range(QS)]

        block = ctx.enter_context(nc.Block())

        def known(turn):
            return isinstance(turn, int)

        def turns(eng, body):
            body(0)
            with eng.Fori(1, TURNS) as turn:
                body(turn)

        @block.gpsimd
        def _(pool):
            nc.gpsimd.memset(ident[:, :], 0.0).then_inc(ident_zeroed, 1)
            pool.wait_ge(ident_zeroed, 1)
            nc.gpsimd.affine_select(out=ident[:, :], in_=ident[:, :], compare_op=ALU.not_equal, fill=1.0,
                                    base=0, pattern=[[-1, P]], channel_multiplier=1).then_inc(ident_ready, 1)

        @block.sync
        def _(sp):
            def body(turn):
                for k in range(BODY):
                    if not (known(turn) and k < XS):
                        sp.wait_ge(transposed, 2 * (turn * BODY + k - XS + 1))
                    sp.dma_start(x_sb[:, k % XS, :], x_units[turn * BODY + k]).then_inc(loaded[k % XS], 16)

            turns(sp, body)

        @block.tensor
        def _(pe):
            def transpose_half(turn, k2):
                k, half = k2 // 2, k2 % 2
                if half == 0:
                    pe.wait_ge(loaded[k % XS], 16 * (turn * (BODY // XS) + k // XS + 1))
                if not (known(turn) and turn * 2 * BODY + k2 < TS):
                    pe.wait_ge(moved, turn * 2 * BODY + k2 - TS + 1)
                for t in range(TH):
                    c = (half * TH + t) * D
                    last = nc.tensor.transpose(xt_ps[:, k2 % TS, t, :], x_sb[:, k % XS, c:c + D], ident[:, :])
                last.then_inc(transposed, 1)

            def gram_unit(turn, k):
                pe.wait_ge(moved, 2 * (turn * BODY + k + 1))
                if k % GU == 0 and not (known(turn) and turn * BODY + k == 0):
                    pe.wait_ge(swapped, turn * BG + k // GU)
                for m in range(PAIRS):
                    for h in range(2):
                        xb = xt_sb[:, k % XTS, (2 * m + h) * F:(2 * m + h + 1) * F]
                        last = nc.tensor.matmul(gram_ps[h * F:(h + 1) * F, k % GU * PAIRS + m, :], xb, xb,
                                                start=True, stop=True)
                last.then_inc(grams, 1)

            def group(turn, g, final=False):
                for u in range(GU):
                    for ahead in range(AHEAD[u], AHEAD[u + 1]):
                        k2 = 2 * g * GU + ahead
                        if k2 < 2 * BODY:
                            transpose_half(turn, k2)
                        elif not final:
                            transpose_half(turn + 1, k2 - 2 * BODY)
                    gram_unit(turn, g * GU + u)

            pe.wait_ge(ident_ready, 1)
            for k2 in range(AHEAD[0]):
                transpose_half(0, k2)
            for g in range(BG):
                group(0, g)
            with pe.Fori(1, TURNS - 1) as turn:
                for g in range(BG):
                    group(turn, g)
            for g in range(BG):
                group(TURNS - 1, g, final=True)

        @block.scalar
        def _(act):
            def move_half(turn, k2):
                act.wait_ge(transposed, turn * 2 * BODY + k2 + 1)
                k, half = k2 // 2, k2 % 2
                if half == 0 and not (known(turn) and turn * BODY + k < XTS):
                    act.wait_ge(grams, turn * BODY + k - XTS + 1)
                nc.scalar.copy(xt_sb[:, k % XTS, :].rearrange("d (c t) -> d t c", t=FPP)[:, half * TH:(half + 1) * TH, :],
                               xt_ps[:, k2 % TS, :, :]).then_inc(moved, 1)

            def store(turn, s, g0, g1):
                for h in range(2):
                    for p0, rows, cols in ((0, upper, slice(0, N0)), (HF, lower, slice(N0, NOUT))):
                        p0 += h * F
                        act.dma_start(out_stores[turn * BS + s, h, :, g0:g1, cols],
                                      rows[p0:p0 + BLK, s, g0:g1, :]).then_inc(stored[s], 16)

            def body(turn):
                for k in range(BODY):
                    for half in range(2):
                        move_half(turn, 2 * k + half)
                    if k % SU == SU // 2 and not (known(turn) and turn == 0):
                        act.wait_ge(packed, ((turn - 1) * BS + k // SU + 1) * NP)
                        store(turn - 1, k // SU, 0, SG)

            turns(act, body)
            act.wait_ge(packed, (STORES - 1) * NP)
            store(TURNS - 1, BS - 2, 0, SG)
            for g in range(SG):
                act.wait_ge(packed, (STORES - 1 + g + 1) * NP)
                store(TURNS - 1, BS - 1, g, g + 1)
            for s in range(QS):
                act.wait_ge(stored[s], 64 * (TURNS + (s == BS - 1) * (SG - 1)))

        @block.vector
        def _(dve):
            def swap_group(turn, g):
                dve.wait_ge(grams, (turn * BG + g + 1) * GU)
                s, a = g // SG, g % SG
                if a == 0 and not (known(turn) and turn == 0):
                    dve.wait_ge(packed, (turn * BS + s - QS + 1) * NP)
                nc.vector.transpose(square[:, s, a, :].rearrange("p (i j) -> p j i", j=F),
                                    gram_ps.rearrange("p b j -> p j b")).then_inc(swapped, 1)

            def pack(turn, s, g0, g1, lo, hi, base):
                for piece in range(lo, hi):
                    half, i, count = PIECES[piece]
                    rows, j0 = ((upper, 0), (lower, HF))[half]
                    if not (known(turn) and turn * BS + s == 0 and piece < 2):
                        dve.wait_ge(packed, base + piece - 1)
                    n = F - 1 - j0 - i
                    at = sum(F - 1 - j0 - r for r in range(i))
                    start = i * F + j0 + i + 1
                    if count == 1:
                        src = square[:, s, g0:g1, start:start + n]
                        dst = rows[:, s, g0:g1, at:at + n]
                    else:
                        src = square[:, s, g0:g1, start:start + 2 * (F + 1)].rearrange(
                            "p a (r j) -> p a r j", r=2)[:, :, :, 0:n]
                        dst = rows[:, s, g0:g1, at:at + 2 * n].rearrange("p a (r j) -> p a r j", r=2)
                    nc.vector.tensor_copy(dst, src).then_inc(packed, 1)

            def pack_part(turn, s, part):
                if part == 0:
                    dve.wait_ge(swapped, (turn * BS + s + 1) * SG)
                    if not (known(turn) and turn == 0):
                        dve.wait_ge(stored[s], turn * 64)
                pack(turn, s, 0, SG, part * NP // SG, (part + 1) * NP // SG, (turn * BS + s) * NP)

            def body(turn):
                for g in range(BG):
                    swap_group(turn, g)
                    if g >= SG:
                        pack_part(turn, g // SG - 1, g % SG)
                    elif not (known(turn) and turn == 0):
                        pack_part(turn - 1, BS - 1, g % SG)

            body(0)
            with dve.Fori(1, TURNS - 1) as turn:
                body(turn)
            swap_group(TURNS - 1, 0)
            pack_part(TURNS - 2, BS - 1, 0)
            swap_group(TURNS - 1, 1)
            pack_part(TURNS - 2, BS - 1, 1)
            swap_group(TURNS - 1, 2)
            pack_part(TURNS - 1, 0, 0)
            pack_part(TURNS - 1, 0, 1)
            dve.wait_ge(swapped, STORES * SG - 1)
            dve.wait_ge(stored[1], (TURNS - 1) * 64)
            pack(TURNS - 1, 1, 0, 1, 0, NP, (STORES - 1) * NP)
            swap_group(TURNS - 1, 3)
            dve.wait_ge(swapped, STORES * SG)
            pack(TURNS - 1, 1, 1, 2, 0, NP, STORES * NP)


_IN = "r_x"


def kernel(**inputs):
    import numpy as np
    import concourse.bacc as bacc
    from concourse import mybir
    from concourse.bass_utils import run_bass_kernel_spmd

    a = np.ascontiguousarray(inputs[_IN])
    batches, features, _ = a.shape
    nc = bacc.Bacc("TRN2", target_bir_lowering=False, num_devices=1)
    x = nc.dram_tensor("x", a.shape, mybir.dt.float32, kind="ExternalInput").ap()
    out = nc.dram_tensor("out", (batches, features * (features - 1) // 2), mybir.dt.float32,
                         kind="ExternalOutput").ap()
    build(nc, x, out)
    r = run_bass_kernel_spmd(nc, [{"x": a}], core_ids=[0])
    return r.results[0]["out"]
```

```python
def build(nc, x, out):
    import concourse.mybir as mybir
    from contextlib import ExitStack

    fp32 = mybir.dt.float32
    ALU = mybir.AluOpType
    P = 128
    BLK = 32
    B, F, D = x.shape
    NOUT = out.shape[1]
    FPP = 8
    UB = P * FPP // F
    PAIRS = UB // 2
    UNITS = B // UB
    GU = BLK // PAIRS
    SG = 4
    LAST = SG // 2
    SU = SG * GU
    STORES = UNITS // SU
    HF = F // 2
    TH = FPP // 2

    XS, TS, XTS, QS = 8, 4, 8, 2
    BODY = QS * SU
    TURNS = UNITS // BODY
    assert BODY % XS == BODY % XTS == 0 and UNITS == TURNS * BODY
    BG = BODY // GU
    BT = BG * (GU - 1)
    BS = BODY // SU

    NT = GU - 1
    AHEAD = (2, 8, 8, 8, 8)
    assert AHEAD[-1] - AHEAD[0] == 2 * NT

    N0 = sum(F - 1 - i for i in range(HF))
    N1 = NOUT - N0
    PIECES = [(half, i, 2) for i in range(0, HF - 2, 2) for half in (0, 1)]
    PIECES += [(0, HF - 2, 1), (1, HF - 2, 1), (0, HF - 1, 1)]
    NP = len(PIECES)
    LEAD = 2
    NBLK = (P // BLK) ** 2

    x_units = x.rearrange("(u b) (g t) d -> u (b g) (t d)", b=UB, t=FPP)
    out_stores = out.rearrange("(s g b h) n -> s h b g n", g=SG, b=BLK, h=2)

    with ExitStack() as ctx:
        def sb(name, shape):
            return ctx.enter_context(nc.sbuf_tensor(name, shape, fp32))

        def sem(name):
            return ctx.enter_context(nc.semaphore(name))

        x_sb = sb("x_sb", [P, XS, FPP * D])
        xt_sb = sb("xt_sb", [P, XTS, UB * F])
        square = sb("square", [P, QS, SG, HF * F])
        upper = sb("upper", [P, QS, SG, N0])
        lower = sb("lower", [P, QS, SG, N1])
        ident = sb("ident", [P, P])
        xt_ps = ctx.enter_context(nc.psum_tensor("xt_ps", [P, TS, TH, P], fp32))
        gram_ps = ctx.enter_context(nc.psum_tensor("gram_ps", [P, BLK, F], fp32))

        ident_zeroed = sem("ident_zeroed")
        ident_ready = sem("ident_ready")
        loaded = [sem(f"loaded{s}") for s in range(XS)]
        transposed = sem("transposed")
        moved = sem("moved")
        blocked = sem("blocked")
        grams = sem("grams")
        swapped = sem("swapped")
        packed = sem("packed")
        packed_last = sem("packed_last")
        stored = [sem(f"stored{s}") for s in range(QS)]

        block = ctx.enter_context(nc.Block())

        def known(turn):
            return isinstance(turn, int)

        def turns(eng, body):
            body(0)
            with eng.Fori(1, TURNS) as turn:
                body(turn)

        def pack(eng, copy, done, before, s, g0, g1, lo, hi):
            for piece in range(lo, hi):
                half, i, count = PIECES[piece]
                rows, j0 = ((upper, 0), (lower, HF))[half]
                if before is not None:
                    eng.wait_ge(done, before + piece - 1)
                elif piece >= 2:
                    eng.wait_ge(done, piece - 1)
                n = F - 1 - j0 - i
                at = sum(F - 1 - j0 - r for r in range(i))
                start = i * F + j0 + i + 1
                if count == 1:
                    src = square[:, s, g0:g1, start:start + n]
                    dst = rows[:, s, g0:g1, at:at + n]
                else:
                    src = square[:, s, g0:g1, start:start + 2 * (F + 1)].rearrange(
                        "p a (r j) -> p a r j", r=2)[:, :, :, 0:n]
                    dst = rows[:, s, g0:g1, at:at + 2 * n].rearrange("p a (r j) -> p a r j", r=2)
                copy(dst, src).then_inc(done, 1)

        @block.gpsimd
        def _(pool):
            nc.gpsimd.memset(ident[:, :], 0.0).then_inc(ident_zeroed, 1)
            pool.wait_ge(ident_zeroed, 1)
            nc.gpsimd.affine_select(out=ident[:, :], in_=ident[:, :], compare_op=ALU.not_equal, fill=1.0,
                                    base=0, pattern=[[-1, P]], channel_multiplier=1).then_inc(ident_ready, 1)

        @block.sync
        def _(sp):
            def body(turn):
                for k in range(BODY):
                    if not (known(turn) and k < XS):
                        g, u = (k - XS) // GU, k % GU
                        if u < NT:
                            sp.wait_ge(transposed, 2 * (turn * BT + g * NT + u + 1))
                        else:
                            sp.wait_ge(blocked, (turn * BG + g + 1) * NBLK)
                    sp.dma_start(x_sb[:, k % XS, :], x_units[turn * BODY + k]).then_inc(loaded[k % XS], 16)

            turns(sp, body)

        @block.tensor
        def _(pe):
            def transpose_half(turn, k2):
                k, half = k2 // 2 // NT * GU + k2 // 2 % NT, k2 % 2
                if half == 0:
                    pe.wait_ge(loaded[k % XS], 16 * (turn * (BODY // XS) + k // XS + 1))
                if not (known(turn) and turn * 2 * BT + k2 < TS):
                    pe.wait_ge(moved, turn * 2 * BT + k2 - TS + 1)
                for t in range(TH):
                    c = (half * TH + t) * D
                    last = nc.tensor.transpose(xt_ps[:, k2 % TS, t, :], x_sb[:, k % XS, c:c + D], ident[:, :])
                last.then_inc(transposed, 1)

            def gram_unit(turn, k):
                g, u = k // GU, k % GU
                if u < NT:
                    pe.wait_ge(moved, 2 * (turn * BT + g * NT + u + 1))
                else:
                    pe.wait_ge(blocked, (turn * BG + g + 1) * NBLK)
                if k % GU == 0 and not (known(turn) and turn * BODY + k == 0):
                    pe.wait_ge(swapped, turn * BG + k // GU)
                for m in range(PAIRS):
                    for h in range(2):
                        xb = xt_sb[:, k % XTS, (2 * m + h) * F:(2 * m + h + 1) * F]
                        last = nc.tensor.matmul(gram_ps[h * F:(h + 1) * F, k % GU * PAIRS + m, :], xb, xb,
                                                start=True, stop=True)
                last.then_inc(grams, 1)

            def group(turn, g, final=False):
                for u in range(GU):
                    for ahead in range(AHEAD[u], AHEAD[u + 1]):
                        k2 = 2 * g * NT + ahead
                        if k2 < 2 * BT:
                            transpose_half(turn, k2)
                        elif not final:
                            transpose_half(turn + 1, k2 - 2 * BT)
                    gram_unit(turn, g * GU + u)

            pe.wait_ge(ident_ready, 1)
            for k2 in range(AHEAD[0]):
                transpose_half(0, k2)
            for g in range(BG):
                group(0, g)
            with pe.Fori(1, TURNS - 1) as turn:
                for g in range(BG):
                    group(turn, g)
            for g in range(BG):
                group(TURNS - 1, g, final=True)

        @block.scalar
        def _(act):
            def move_half(turn, k, half):
                act.wait_ge(transposed, 2 * (turn * BT + k // GU * NT + k % GU) + half + 1)
                k2 = 2 * (k // GU * NT + k % GU) + half
                if half == 0 and not (known(turn) and turn * BODY + k < XTS):
                    act.wait_ge(grams, turn * BODY + k - XTS + 1)
                nc.scalar.copy(xt_sb[:, k % XTS, :].rearrange("d (c t) -> d t c", t=FPP)[:, half * TH:(half + 1) * TH, :],
                               xt_ps[:, k2 % TS, :, :]).then_inc(moved, 1)

            def pack_part(turn, s, part):
                if part == 0:
                    act.wait_ge(swapped, (turn * BS + s + 1) * SG)
                    if not (known(turn) and turn == 0):
                        act.wait_ge(stored[s], turn * 64)
                before = None if known(turn) and turn == 0 and s == 0 else (turn * BS + s) * NP
                pack(act, nc.scalar.copy, packed, before, s, 0, SG, part * NP // SG, (part + 1) * NP // SG)

            def store_half(turn, s, g0, g1, half):
                p0, rows, cols = ((0, upper, slice(0, N0)), (HF, lower, slice(N0, NOUT)))[half]
                for h in range(2):
                    q0 = h * F + p0
                    act.dma_start(out_stores[turn * BS + s, h, :, g0:g1, cols],
                                  rows[q0:q0 + BLK, s, g0:g1, :]).then_inc(stored[s], 16)

            def store(turn, s, g0, g1, pieces):
                act.wait_ge(packed, pieces)
                for half in range(2):
                    store_half(turn, s, g0, g1, half)

            def body(turn):
                for g in range(BG):
                    for u in range(NT):
                        for half in range(2):
                            move_half(turn, g * GU + u, half)
                    s, part = g // SG, g % SG
                    if part == 0 and not (known(turn) and turn == 0):
                        store(turn - 1, s, 0, SG, (turn * BS + s - 1) * NP)
                    if s > 0:
                        pack_part(turn, s - 1, part)
                    elif not (known(turn) and turn == 0):
                        pack_part(turn - 1, BS - 1, part)

            turns(act, body)
            t, s = TURNS - 1, BS - 1
            store(t, s - 1, 0, SG, (STORES - 1) * NP)
            act.wait_ge(stored[s], t * 64)
            pack(act, nc.scalar.copy, packed, (STORES - 1) * NP, s, 0, LAST, 0, NP)
            store(t, s, 0, LAST, STORES * NP)
            act.wait_ge(packed_last, NP)
            for half in range(2):
                store_half(t, s, LAST, SG, half)
            for s in range(QS):
                act.wait_ge(stored[s], 64 * (TURNS + (s == BS - 1)))

        @block.vector
        def _(dve):
            def swap_group(turn, g):
                dve.wait_ge(grams, (turn * BG + g + 1) * GU)
                s, a = g // SG, g % SG
                if a == 0 and not (known(turn) and turn == 0):
                    dve.wait_ge(packed, (turn * BS + s - QS + 1) * NP)
                nc.vector.transpose(square[:, s, a, :].rearrange("p (i j) -> p j i", j=F),
                                    gram_ps.rearrange("p b j -> p j b")).then_inc(swapped, 1)

            def block_unit(turn, g):
                k = g * GU + GU - 1
                dve.wait_ge(loaded[k % XS], 16 * (turn * (BODY // XS) + k // XS + 1))
                if not (known(turn) and turn * BODY + k < XTS):
                    dve.wait_ge(grams, turn * BODY + k - XTS + 1)
                for r in range(P // BLK):
                    for c in range(P // BLK):
                        src = x_sb[r * BLK:(r + 1) * BLK, k % XS, :].rearrange("b (t d) -> b t d", t=FPP)
                        dst = xt_sb[c * BLK:(c + 1) * BLK, k % XTS, r * BLK * FPP:(r + 1) * BLK * FPP]
                        nc.vector.transpose(dst.rearrange("d (b t) -> d t b", t=FPP),
                                            src[:, :, c * BLK:(c + 1) * BLK]).then_inc(blocked, 1)

            def body(turn):
                for g in range(BG):
                    swap_group(turn, g)
                    if g + LEAD < BG:
                        block_unit(turn, g + LEAD)
                    else:
                        block_unit(turn + 1, g + LEAD - BG)

            for g in range(LEAD):
                block_unit(0, g)
            body(0)
            with dve.Fori(1, TURNS - 1) as turn:
                body(turn)
            for g in range(BG):
                swap_group(TURNS - 1, g)
                if g + LEAD < BG:
                    block_unit(TURNS - 1, g + LEAD)
            dve.wait_ge(swapped, STORES * SG)
            dve.wait_ge(stored[BS - 1], (TURNS - 1) * 64)
            pack(dve, nc.vector.tensor_copy, packed_last, None, BS - 1, LAST, SG, 0, NP)


_IN = "r_x"


def kernel(**inputs):
    import numpy as np
    import concourse.bacc as bacc
    from concourse import mybir
    from concourse.bass_utils import run_bass_kernel_spmd

    a = np.ascontiguousarray(inputs[_IN])
    batches, features, _ = a.shape
    nc = bacc.Bacc("TRN2", target_bir_lowering=False, num_devices=1)
    x = nc.dram_tensor("x", a.shape, mybir.dt.float32, kind="ExternalInput").ap()
    out = nc.dram_tensor("out", (batches, features * (features - 1) // 2), mybir.dt.float32,
                         kind="ExternalOutput").ap()
    build(nc, x, out)
    r = run_bass_kernel_spmd(nc, [{"x": a}], core_ids=[0])
    return r.results[0]["out"]
```
